# Optimizing a Trainium2 kernel written in Bass

```python
import numpy as np
import jax
import jax.numpy as jnp

def _softmax(x, axis=-1):
    return jax.nn.softmax(x, axis=axis)

def _gelu(x):
    return jax.nn.gelu(x, approximate=True)

def _silu(x):
    return jax.nn.silu(x)

def _sigmoid(x):
    return jax.nn.sigmoid(x)

def _layernorm(x, axis=-1, eps=1e-05):
    m = jnp.mean(x, axis=axis, keepdims=True)
    v = jnp.var(x, axis=axis, keepdims=True)
    return (x - m) / jnp.sqrt(v + eps)

def _scatter_add(tgt, idx, src, axis=0):
    return tgt.at[idx].add(src)

def _segment_sum(src, seg, n):
    return jax.ops.segment_sum(src, seg, n)
kernel_name = 'mk_dlrm_tower_d1_rec_r8_de08eb'

def setup_inputs(seed: int=0):
    np.random.seed(seed)
    _w = jnp.asarray

    def _rec_inputs():
        import jax
        import jax.numpy as jnp
        _tk = jax.random.key(seed)
        dense_ctx = jax.random.normal(jax.random.fold_in(_tk, 190), (512, 16), jnp.float32)
        ids = jnp.stack([jax.random.randint(jax.random.fold_in(_tk, 200 + f), (512,), 0, v, jnp.int32) for f, v in enumerate([1000, 1250, 1250, 125000, 12500, 1000, 12500, 12500, 12500, 12500, 1250, 1000, 1000, 1000, 1250, 12500, 1250, 1250, 1250, 12500, 12500, 1000, 1000, 1000, 1250, 1250, 1000, 1000, 1000, 1250, 1250, 1250])], axis=1)
        tbl_0 = 0.05 * jax.random.normal(jax.random.fold_in(_tk, 500 + 0), (1000, 128), jnp.float32)
        tbl_1 = 0.05 * jax.random.normal(jax.random.fold_in(_tk, 500 + 1), (1250, 128), jnp.float32)
        tbl_2 = 0.05 * jax.random.normal(jax.random.fold_in(_tk, 500 + 2), (1250, 128), jnp.float32)
        tbl_3 = 0.05 * jax.random.normal(jax.random.fold_in(_tk, 500 + 3), (125000, 128), jnp.float32)
        tbl_4 = 0.05 * jax.random.normal(jax.random.fold_in(_tk, 500 + 4), (12500, 128), jnp.float32)
        tbl_5 = 0.05 * jax.random.normal(jax.random.fold_in(_tk, 500 + 5), (1000, 128), jnp.float32)
        tbl_6 = 0.05 * jax.random.normal(jax.random.fold_in(_tk, 500 + 6), (12500, 128), jnp.float32)
        tbl_7 = 0.05 * jax.random.normal(jax.random.fold_in(_tk, 500 + 7), (12500, 128), jnp.float32)
        tbl_8 = 0.05 * jax.random.normal(jax.random.fold_in(_tk, 500 + 8), (12500, 128), jnp.float32)
        tbl_9 = 0.05 * jax.random.normal(jax.random.fold_in(_tk, 500 + 9), (12500, 128), jnp.float32)
        tbl_10 = 0.05 * jax.random.normal(jax.random.fold_in(_tk, 500 + 10), (1250, 128), jnp.float32)
        tbl_11 = 0.05 * jax.random.normal(jax.random.fold_in(_tk, 500 + 11), (1000, 128), jnp.float32)
        tbl_12 = 0.05 * jax.random.normal(jax.random.fold_in(_tk, 500 + 12), (1000, 128), jnp.float32)
        tbl_13 = 0.05 * jax.random.normal(jax.random.fold_in(_tk, 500 + 13), (1000, 128), jnp.float32)
        tbl_14 = 0.05 * jax.random.normal(jax.random.fold_in(_tk, 500 + 14), (1250, 128), jnp.float32)
        tbl_15 = 0.05 * jax.random.normal(jax.random.fold_in(_tk, 500 + 15), (12500, 128), jnp.float32)
        tbl_16 = 0.05 * jax.random.normal(jax.random.fold_in(_tk, 500 + 16), (1250, 128), jnp.float32)
        tbl_17 = 0.05 * jax.random.normal(jax.random.fold_in(_tk, 500 + 17), (1250, 128), jnp.float32)
        tbl_18 = 0.05 * jax.random.normal(jax.random.fold_in(_tk, 500 + 18), (1250, 128), jnp.float32)
        tbl_19 = 0.05 * jax.random.normal(jax.random.fold_in(_tk, 500 + 19), (12500, 128), jnp.float32)
        tbl_20 = 0.05 * jax.random.normal(jax.random.fold_in(_tk, 500 + 20), (12500, 128), jnp.float32)
        tbl_21 = 0.05 * jax.random.normal(jax.random.fold_in(_tk, 500 + 21), (1000, 128), jnp.float32)
        tbl_22 = 0.05 * jax.random.normal(jax.random.fold_in(_tk, 500 + 22), (1000, 128), jnp.float32)
        tbl_23 = 0.05 * jax.random.normal(jax.random.fold_in(_tk, 500 + 23), (1000, 128), jnp.float32)
        tbl_24 = 0.05 * jax.random.normal(jax.random.fold_in(_tk, 500 + 24), (1250, 128), jnp.float32)
        tbl_25 = 0.05 * jax.random.normal(jax.random.fold_in(_tk, 500 + 25), (1250, 128), jnp.float32)
        tbl_26 = 0.05 * jax.random.normal(jax.random.fold_in(_tk, 500 + 26), (1000, 128), jnp.float32)
        tbl_27 = 0.05 * jax.random.normal(jax.random.fold_in(_tk, 500 + 27), (1000, 128), jnp.float32)
        tbl_28 = 0.05 * jax.random.normal(jax.random.fold_in(_tk, 500 + 28), (1000, 128), jnp.float32)
        tbl_29 = 0.05 * jax.random.normal(jax.random.fold_in(_tk, 500 + 29), (1250, 128), jnp.float32)
        tbl_30 = 0.05 * jax.random.normal(jax.random.fold_in(_tk, 500 + 30), (1250, 128), jnp.float32)
        tbl_31 = 0.05 * jax.random.normal(jax.random.fold_in(_tk, 500 + 31), (1250, 128), jnp.float32)
        _rk = jax.random.fold_in(_tk, 7)
        W_top1 = 0.0441942 * jax.random.normal(jax.random.fold_in(_tk, 801), (512, 512), jnp.float32)
        W_top2 = 0.0441942 * jax.random.normal(jax.random.fold_in(_tk, 802), (512, 256), jnp.float32)
        W_top3 = 0.0625 * jax.random.normal(jax.random.fold_in(_tk, 803), (256, 1), jnp.float32)
        b_top1 = jnp.zeros((512,), jnp.float32)
        b_top2 = jnp.zeros((256,), jnp.float32)
        return (dense_ctx, ids, tbl_0, tbl_1, tbl_2, tbl_3, tbl_4, tbl_5, tbl_6, tbl_7, tbl_8, tbl_9, tbl_10, tbl_11, tbl_12, tbl_13, tbl_14, tbl_15, tbl_16, tbl_17, tbl_18, tbl_19, tbl_20, tbl_21, tbl_22, tbl_23, tbl_24, tbl_25, tbl_26, tbl_27, tbl_28, tbl_29, tbl_30, tbl_31, W_top1, b_top1, W_top2, b_top2, W_top3)
    dense_ctx, ids, tbl_0, tbl_1, tbl_2, tbl_3, tbl_4, tbl_5, tbl_6, tbl_7, tbl_8, tbl_9, tbl_10, tbl_11, tbl_12, tbl_13, tbl_14, tbl_15, tbl_16, tbl_17, tbl_18, tbl_19, tbl_20, tbl_21, tbl_22, tbl_23, tbl_24, tbl_25, tbl_26, tbl_27, tbl_28, tbl_29, tbl_30, tbl_31, W_top1, b_top1, W_top2, b_top2, W_top3 = _rec_inputs()

    def _L0_rec_setup():
        import jax, jax.numpy as jnp
        import numpy as np
        N_FEATS = 32
        EMBED_D = 128
        BATCH = 2048
        SELF_INTERACTION = False
        key = jax.random.key(seed)
        x = jax.random.normal(key, (BATCH, N_FEATS, EMBED_D), dtype=jnp.float32)
        return {'x': x}
    _L0_rec_all = _L0_rec_setup()
    _L0_rec_in = {k: v for k, v in _L0_rec_all.items() if k in ()}
    del _L0_rec_all
    return {'dense_ctx': dense_ctx, 'ids': ids, 'tbl_0': tbl_0, 'tbl_1': tbl_1, 'tbl_2': tbl_2, 'tbl_3': tbl_3, 'tbl_4': tbl_4, 'tbl_5': tbl_5, 'tbl_6': tbl_6, 'tbl_7': tbl_7, 'tbl_8': tbl_8, 'tbl_9': tbl_9, 'tbl_10': tbl_10, 'tbl_11': tbl_11, 'tbl_12': tbl_12, 'tbl_13': tbl_13, 'tbl_14': tbl_14, 'tbl_15': tbl_15, 'tbl_16': tbl_16, 'tbl_17': tbl_17, 'tbl_18': tbl_18, 'tbl_19': tbl_19, 'tbl_20': tbl_20, 'tbl_21': tbl_21, 'tbl_22': tbl_22, 'tbl_23': tbl_23, 'tbl_24': tbl_24, 'tbl_25': tbl_25, 'tbl_26': tbl_26, 'tbl_27': tbl_27, 'tbl_28': tbl_28, 'tbl_29': tbl_29, 'tbl_30': tbl_30, 'tbl_31': tbl_31, 'W_top1': W_top1, 'b_top1': b_top1, 'W_top2': W_top2, 'b_top2': b_top2, 'W_top3': W_top3}

def reference(dense_ctx, ids, tbl_0, tbl_1, tbl_2, tbl_3, tbl_4, tbl_5, tbl_6, tbl_7, tbl_8, tbl_9, tbl_10, tbl_11, tbl_12, tbl_13, tbl_14, tbl_15, tbl_16, tbl_17, tbl_18, tbl_19, tbl_20, tbl_21, tbl_22, tbl_23, tbl_24, tbl_25, tbl_26, tbl_27, tbl_28, tbl_29, tbl_30, tbl_31, W_top1, b_top1, W_top2, b_top2, W_top3):
    import jax
    import jax.numpy as jnp

    def _L0_rec_ref(x):
        import jax, jax.numpy as jnp
        import numpy as np
        N_FEATS = 32
        EMBED_D = 128
        BATCH = 2048
        SELF_INTERACTION = False
        B, N, D = x.shape
        dot = jnp.einsum('bnd,bmd->bnm', x, x)
        k = 0 if SELF_INTERACTION else 1
        iu, ju = jnp.triu_indices(N, k=k)
        flat = dot[:, iu, ju]
        return flat
    e = jnp.stack([tbl_0[ids[:, 0]], tbl_1[ids[:, 1]], tbl_2[ids[:, 2]], tbl_3[ids[:, 3]], tbl_4[ids[:, 4]], tbl_5[ids[:, 5]], tbl_6[ids[:, 6]], tbl_7[ids[:, 7]], tbl_8[ids[:, 8]], tbl_9[ids[:, 9]], tbl_10[ids[:, 10]], tbl_11[ids[:, 11]], tbl_12[ids[:, 12]], tbl_13[ids[:, 13]], tbl_14[ids[:, 14]], tbl_15[ids[:, 15]], tbl_16[ids[:, 16]], tbl_17[ids[:, 17]], tbl_18[ids[:, 18]], tbl_19[ids[:, 19]], tbl_20[ids[:, 20]], tbl_21[ids[:, 21]], tbl_22[ids[:, 22]], tbl_23[ids[:, 23]], tbl_24[ids[:, 24]], tbl_25[ids[:, 25]], tbl_26[ids[:, 26]], tbl_27[ids[:, 27]], tbl_28[ids[:, 28]], tbl_29[ids[:, 29]], tbl_30[ids[:, 30]], tbl_31[ids[:, 31]]], axis=1)
    z = _L0_rec_ref(e)
    z = z.reshape(z.shape[0], -1)
    h = jnp.concatenate([z, dense_ctx], axis=1)
    h = jnp.maximum(h @ W_top1 + b_top1, 0.0)
    h = jnp.maximum(h @ W_top2 + b_top2, 0.0)
    y = h @ W_top3
    return y

_drawn_inputs = setup_inputs


def setup_inputs(seed=0):
    import zlib

    import numpy as np

    out = dict(_drawn_inputs(seed))
    spreads = {'b_top1': (0.0, 0.1), 'b_top2': (0.0, 0.1)}
    factors = {}
    for name, (base, spread) in spreads.items():
        noise = np.random.default_rng([zlib.crc32(name.encode()), seed]).standard_normal(out[name].shape)
        drawn = base * np.exp(spread * noise) if base else spread * noise
        out[name] = jnp.asarray(drawn.astype(out[name].dtype))
    for name, factor in factors.items():
        out[name] = (out[name] * factor).astype(out[name].dtype)
    return out
```

```python
import concourse.bass as bass
from concourse import mybir
from contextlib import ExitStack

P = 128
B, F, D = 512, 32, 128
RB = 64
ROUNDS = B // RB
UNITS = 4
UB = RB // UNITS
ROWS = [1000, 1250, 1250, 125000, 12500, 1000, 12500, 12500, 12500, 12500, 1250, 1000, 1000, 1000,
        1250, 12500, 1250, 1250, 1250, 12500, 12500, 1000, 1000, 1000, 1250, 1250, 1000, 1000,
        1000, 1250, 1250, 1250]
PICK = 8
PICK_ROWS = 1000
PICKED = [f for f in range(F) if ROWS[f] == PICK_ROWS][:PICK]
SLOTS = [f for f in range(F) if f not in PICKED] + PICKED
GF = F - PICK
G0 = UB * F // P
G = UB * GF // P
KP = 125
KR = PICK_ROWS // KP
PARTS = 3
JQ, JC = 4, 8
CTX = 16
H1, H2 = 512, 256
N1, N2 = H1 // P, H2 // P
IDS0, IDS = 0, UNITS * G0
IDCOLS = IDS + (ROUNDS - 1) * UNITS * G


def build(nc, row_ids, starts, pick_ids, tables, picked, dense_t, w1, w2, small, y):
    f32, bf16, i32 = mybir.dt.float32, mybir.dt.bfloat16, mybir.dt.int32
    ALU = mybir.AluOpType
    ACT = mybir.ActivationFunctionType
    ctx = ExitStack()
    with ctx:
        def sb(name, shape, dt):
            return ctx.enter_context(nc.sbuf_tensor(name, shape, dt))

        def pb(name, shape):
            return ctx.enter_context(nc.psum_tensor(name, shape, f32))

        def sem(name):
            return ctx.enter_context(nc.semaphore(name))

        ident = sb("ident", [P, P], f32)
        gate = sb("gate", [1, 3], f32)
        id_sb = sb("id_sb", [P, IDCOLS], i32)
        start_sb = sb("start_sb", [P, UNITS * (G0 + G)], f32)
        row_no = sb("row_no", [P, 2, UNITS * G0], i32)
        rows = sb("rows", [P, 2, UNITS * G0, D], f32)
        emb = sb("emb", [P, 2, RB, F], f32)
        pick_id_sb = sb("pick_id_sb", [KP, PICK, B], i32)
        pick_row = sb("pick_row", [KP, KR], i32)
        onehot = sb("onehot", [KP, 2, PICK, KR, RB], bf16)
        table = sb("table", [KP, PICK, KR * D], f32)
        part = sb("part", [KP, PARTS, PICK, KR * D], bf16)
        feat = sb("feat", [P, JC, B], f32)
        w1_sb = sb("w1_sb", [P, JC, H1], f32)
        w2_sb = sb("w2_sb", [P, N1, H2], f32)
        small_sb = sb("small_sb", [P, N1 + 2 * N2], f32)
        h1 = sb("h1", [P, N1, RB], f32)
        h2 = sb("h2", [P, N2, RB], f32)
        y_row = sb("y_row", [1, B], f32)
        b1 = small_sb[:, 0:N1]
        b2 = small_sb[:, N1:N1 + N2]
        w3 = small_sb[:, N1 + N2:N1 + 2 * N2]

        turn_ps = [pb(f"turn_ps{i}", [P, 512]) for i in range(2)]
        dot_ps = [pb(f"dot_ps{i}", [P, RB // 4, F]) for i in range(2)]
        pick_ps = pb("pick_ps", [P, PICK, RB])
        h1_ps = [pb(f"h1_ps{i}", [P, N1 // 2, RB]) for i in range(2)]
        h2_ps = pb("h2_ps", [P, 512])

        ids_in = sem("ids_in")
        pick_ids_in = sem("pick_ids_in")
        table_in = [sem(f"table_in{t}") for t in range(PICK)]
        weights_in = sem("weights_in")
        rows_in = [[sem(f"rows_in{p}_{u}") for u in range(UNITS)] for p in range(2)]
        stored = sem("stored")
        ident_ready = sem("ident_ready")
        pick_row_ready = sem("pick_row_ready")
        zeroed = sem("zeroed")
        row_no_ready = sem("row_no_ready")
        gate_passed = sem("gate_passed")
        hi_ready = sem("hi_ready")
        rest_ready = sem("rest_ready")
        mid_ready = sem("mid_ready")
        lo_ready = sem("lo_ready")
        turned = sem("turned")
        emb_ready = sem("emb_ready")
        onehot_ready = sem("onehot_ready")
        picked_done = sem("picked_done")
        pick_emb_ready = sem("pick_emb_ready")
        dots = sem("dots")
        feat_act = sem("feat_act")
        feat_dve = sem("feat_dve")
        h1_done = sem("h1_done")
        h1_act = sem("h1_act")
        h1_dve = sem("h1_dve")
        h2_done = sem("h2_done")
        h2_ready = sem("h2_ready")
        y_done = sem("y_done")
        y_copied = sem("y_copied")

        feat_v = feat[:, :, :].rearrange("p c (g s) -> p c g s", s=4)

        def gathers(first):
            return G0 if first else G

        def copy_dots(copy, r, par, quads):
            last = None
            for s in quads:
                for q in range(JQ):
                    n = 16 if q == 0 else 32
                    src = dot_ps[par][32 * s:32 * s + n, :, JC * q:JC * (q + 1)]
                    last = copy(feat_v[32 * q:32 * q + n, :, bass.ds(r * (RB // 4), RB // 4), s],
                                src.rearrange("p g c -> p c g"))
            return last

        block = ctx.enter_context(nc.Block())

        @block.sync
        def _(sp):
            sp.dma_start(id_sb[:, :], row_ids).then_inc(ids_in, 16)
            sp.dma_start(start_sb[:, :], starts).then_inc(ids_in, 16)
            for t in range(2):
                sp.dma_start(table[:, t, :], picked[t]).then_inc(table_in[t], 16)
            sp.dma_start(pick_id_sb[:, :, :].rearrange("p t b -> p (t b)"),
                         pick_ids.broadcast_to([KP, PICK * B])).then_inc(pick_ids_in, 16)
            for t in range(2, PICK):
                sp.dma_start(table[:, t, :], picked[t]).then_inc(table_in[t], 16)
            sp.dma_start(feat[16:16 + CTX, 0, :], dense_t).then_inc(weights_in, 16)
            sp.dma_start(small_sb[:, :], small).then_inc(weights_in, 16)
            sp.dma_start(w1_sb[:, :, :], w1).then_inc(weights_in, 16)
            sp.dma_start(w2_sb[:, :, :], w2.rearrange("(c p) n -> p c n", p=P)).then_inc(weights_in, 16)
            sp.wait_ge(y_copied, ROUNDS)
            sp.dma_start(y.rearrange("b o -> o b"), y_row[:, :]).then_inc(stored, 16)
            sp.wait_ge(stored, 16)

        @block.gpsimd
        def _(pool):
            def gather_round(r, par, first=False):
                pool.wait_ge(row_no_ready, r + 1)
                pool.tensor_tensor(gate[:, par:par + 1], gate[:, 2:3], gate[:, 2:3],
                                   ALU.add).then_inc(gate_passed, 1)
                n = gathers(first)
                for u in range(UNITS):
                    for c in range(n):
                        pool.indirect_dma_start(
                            rows[:, par, n * u + c, :], None, tables,
                            bass.IndirectOffsetOnAxis(ap=row_no[:, par, n * u + c:n * u + c + 1], axis=0)
                        ).then_inc(rows_in[par][u], 16)

            pool.memset(ident[:, :], 0.0).then_inc(ident_ready, 1)
            pool.iota(pick_row[:, :], [[1, KR]], base=0, channel_multiplier=KR).then_inc(pick_row_ready, 1)
            pool.memset(gate[:, :], 0.0).then_inc(ident_ready, 1)
            pool.wait_ge(ident_ready, 2)
            pool.affine_select(out=ident[:, :], in_=ident[:, :], compare_op=ALU.not_equal, fill=1.0,
                               base=0, pattern=[[-1, P]], channel_multiplier=1).then_inc(ident_ready, 1)
            gather_round(0, 0, first=True)
            with pool.Fori(1, ROUNDS - 1, 2) as r:
                gather_round(r, 1)
                gather_round(r + 1, 0)
            gather_round(ROUNDS - 1, 1)

        @block.vector
        def _(dve):
            def row_numbers(r, par, first=False, fresh=False):
                if first:
                    src, at, n = id_sb[:, IDS0:IDS0 + UNITS * G0], 0, UNITS * G0
                else:
                    src = id_sb[:, bass.ds(IDS + (r - 1) * (UNITS * G), UNITS * G)]
                    at, n = UNITS * G0, UNITS * G
                if not fresh:
                    dve.wait_ge(gate_passed, r - 1)
                dve.tensor_tensor(row_no[:, par, 0:n], src, start_sb[:, at:at + n],
                                  ALU.add).then_inc(row_no_ready, 1)

            def rest_parts(t):
                dve.wait_ge(hi_ready, t + 1)
                dve.tensor_tensor(table[:, t, :], table[:, t, :], part[:, 0, t, :],
                                  ALU.subtract).then_inc(rest_ready, 1)

            def low_part(t):
                dve.wait_ge(mid_ready, t + 1)
                dve.tensor_tensor(part[:, 2, t, :], table[:, t, :], part[:, 1, t, :],
                                  ALU.subtract).then_inc(lo_ready, 1)

            def make_onehot(r, par, half):
                n = PICK // 2
                ts = slice(n * half, n * half + n)
                ids = pick_id_sb[:, ts, bass.ds(r * RB, RB)]
                dve.tensor_tensor(onehot[:, par, ts, :, :],
                                  ids.unsqueeze(2).broadcast_to([KP, n, KR, RB]),
                                  pick_row[:, :].unsqueeze(1).unsqueeze(3).broadcast_to([KP, n, KR, RB]),
                                  ALU.is_equal).then_inc(onehot_ready, 1)

            def h1_relu(r):
                dve.wait_ge(h1_done, r + 1)
                for n in range(N1 // 2, N1):
                    last = dve.tensor_scalar(h1[:, n, :], h1_ps[1][:, n - N1 // 2, :], b1[:, n:n + 1], 0.0,
                                             ALU.add, ALU.max)
                last.then_inc(h1_dve, 1)

            def h2_relu(r):
                dve.wait_ge(h2_done, r + 1)
                for n in range(N2):
                    last = dve.tensor_scalar(h2[:, n, :], h2_ps[:, n * RB:(n + 1) * RB], b2[:, n:n + 1], 0.0,
                                             ALU.add, ALU.max)
                last.then_inc(h2_ready, 1)

            def dots_out(r, par):
                dve.wait_ge(dots, UNITS * r + UNITS)
                copy_dots(dve.tensor_copy, r, par, (2, 3)).then_inc(feat_dve, 1)

            dve.wait_ge(ids_in, 32)
            row_numbers(0, 0, first=True, fresh=True)
            row_numbers(1, 1, fresh=True)
            dve.memset(feat[0:32, 1:JC, :], 0.0).then_inc(zeroed, 1)
            for t in range(PICK):
                rest_parts(t)
                if t == 1:
                    dve.wait_ge(pick_ids_in, 16)
                    dve.wait_ge(pick_row_ready, 1)
                    make_onehot(1, 1, 0)
                if t == PICK // 2:
                    make_onehot(1, 1, 1)
                if t >= 1:
                    low_part(t - 1)
            low_part(PICK - 1)
            dve.wait_ge(weights_in, 64)
            dots_out(0, 0)
            row_numbers(2, 0)

            def round_(r, par, last=False):
                h1_relu(r - 1)
                if not last:
                    make_onehot(r + 1, 1 - par, 0)
                h2_relu(r - 1)
                if not last:
                    make_onehot(r + 1, 1 - par, 1)
                dots_out(r, par)

            with dve.Fori(1, ROUNDS - 3, 2) as r:
                for par in (1, 0):
                    round_(r + 1 - par, par)
                    row_numbers(r + 1 - par + 2, par)
            round_(ROUNDS - 3, 1)
            row_numbers(ROUNDS - 1, 1)
            round_(ROUNDS - 2, 0)
            round_(ROUNDS - 1, 1, last=True)
            h1_relu(ROUNDS - 1)
            h2_relu(ROUNDS - 1)

        @block.scalar
        def _(act):
            def hi_part(t):
                act.wait_ge(table_in[t], 16)
                act.activation(part[:, 0, t, :], table[:, t, :], ACT.Copy).then_inc(hi_ready, 1)

            def mid_part(t):
                act.wait_ge(rest_ready, t + 1)
                act.activation(part[:, 1, t, :], table[:, t, :], ACT.Copy).then_inc(mid_ready, 1)

            def emb_out(r, par, u, first=False):
                act.wait_ge(turned, UNITS * r + u + 1)
                n = F if first else GF
                act.activation(emb[:, par, UB * u:UB * (u + 1), 0:n],
                               turn_ps[u % 2][:, 0:UB * n].rearrange("p (b f) -> p b f", f=n),
                               ACT.Copy).then_inc(emb_ready, 1)

            def pick_out(r, par):
                act.wait_ge(picked_done, 2 * r)
                act.activation(emb[:, par, :, GF:F].rearrange("p b t -> p t b"), pick_ps[:, :, :],
                               ACT.Copy).then_inc(pick_emb_ready, 1)

            def dots_out(r, par):
                act.wait_ge(dots, UNITS * r + UNITS)
                copy_dots(lambda o, i: act.activation(o, i, ACT.Copy), r, par, (0, 1)).then_inc(feat_act, 1)

            def h1_relu(r):
                act.wait_ge(h1_done, r + 1)
                for n in range(N1 // 2):
                    last = act.activation(h1[:, n, :], h1_ps[0][:, n, :], ACT.Relu, bias=b1[:, n:n + 1])
                last.then_inc(h1_act, 1)

            def y_out(r):
                act.wait_ge(y_done, r + 1)
                act.activation(y_row[:, bass.ds(r * RB, RB)], h2_ps[0:1, 2 * RB:3 * RB],
                               ACT.Copy).then_inc(y_copied, 1)

            for t in range(PICK):
                hi_part(t)
                if t >= 1:
                    mid_part(t - 1)
                if t % 2 == 1:
                    emb_out(0, 0, t // 2, first=True)
            mid_part(PICK - 1)
            act.wait_ge(zeroed, 1)
            act.wait_ge(weights_in, 64)
            dots_out(0, 0)

            def round_(r, par):
                h1_relu(r - 1)
                pick_out(r, par)
                emb_out(r, par, 0)
                y_out(r - 1)
                for u in range(1, UNITS):
                    emb_out(r, par, u)
                dots_out(r, par)

            with act.Fori(1, ROUNDS - 1, 2) as r:
                round_(r, 1)
                round_(r + 1, 0)
            round_(ROUNDS - 1, 1)
            h1_relu(ROUNDS - 1)
            y_out(ROUNDS - 1)

        @block.tensor
        def _(pe):
            def turn(r, par, u, first=False):
                n = gathers(first)
                landed = 24 * r + (64 if par == 0 else 24)
                pe.wait_ge(rows_in[par][u], landed)
                for c in range(n):
                    last = pe.transpose(turn_ps[u % 2][:, c * P:(c + 1) * P],
                                        rows[:, par, n * u + c, :], ident[:, :])
                last.then_inc(turned, 1)

            def dot(r, par, u):
                pe.wait_ge(emb_ready, UNITS * r + u + 1)
                for b in range(UB * u, UB * (u + 1)):
                    s, g = b % 4, b // 4
                    e = emb[:, par, b, :]
                    last = pe.matmul(dot_ps[par][32 * s:32 * s + 32, g, :], e, e, start=True, stop=True,
                                     tile_position=(0, 32 * s))
                last.then_inc(dots, 1)

            def pick(r, par, half, first=False):
                pe.wait_ge(onehot_ready, 2 * r + half - 1)
                n = PICK // 2
                for t in range(n * half, n * half + n):
                    if first:
                        pe.wait_ge(lo_ready, t + 1)
                    for k in range(KR):
                        for m in range(PARTS):
                            last = pe.matmul(pick_ps[:, t, :], part[:, m, t, D * k:D * (k + 1)],
                                             onehot[:, par, t, k, :], start=(k == 0 and m == 0),
                                             stop=(k == KR - 1 and m == PARTS - 1))
                last.then_inc(picked_done, 1)

            def layer1(r):
                pe.wait_ge(feat_act, r + 1)
                pe.wait_ge(feat_dve, r + 1)
                for n in range(N1):
                    for c in range(JC):
                        last = pe.matmul(h1_ps[n // 2][:, n % 2, :], w1_sb[:, c, n * P:(n + 1) * P],
                                         feat[:, c, bass.ds(r * RB, RB)], start=(c == 0), stop=(c == JC - 1))
                last.then_inc(h1_done, 1)

            def layer2(r):
                pe.wait_ge(h1_act, r + 1)
                pe.wait_ge(h1_dve, r + 1)
                for n in range(N2):
                    for c in range(N1):
                        last = pe.matmul(h2_ps[:, n * RB:(n + 1) * RB], w2_sb[:, c, n * P:(n + 1) * P],
                                         h1[:, c, :], start=(c == 0), stop=(c == N1 - 1))
                last.then_inc(h2_done, 1)

            def layer3(r):
                pe.wait_ge(h2_ready, r + 1)
                for c in range(N2):
                    last = pe.matmul(h2_ps[0:1, 2 * RB:3 * RB], w3[:, c:c + 1], h2[:, c, :],
                                     start=(c == 0), stop=(c == N2 - 1))
                last.then_inc(y_done, 1)

            pe.wait_ge(ident_ready, 3)
            turn(0, 0, 0, first=True)
            turn(0, 0, 1, first=True)
            dot(0, 0, 0)
            turn(0, 0, 2, first=True)
            dot(0, 0, 1)
            pick(1, 1, 0, first=True)
            turn(0, 0, 3, first=True)
            dot(0, 0, 2)
            dot(0, 0, 3)
            pe.wait_ge(weights_in, 64)
            layer1(0)
            pick(1, 1, 1, first=True)
            layer2(0)

            def round_(r, par, last=False):
                turn(r, par, 0)
                layer3(r - 1)
                turn(r, par, 1)
                pe.wait_ge(pick_emb_ready, r)
                dot(r, par, 0)
                turn(r, par, 2)
                dot(r, par, 1)
                turn(r, par, 3)
                dot(r, par, 2)
                dot(r, par, 3)
                if not last:
                    pick(r + 1, 1 - par, 0)
                layer1(r)
                if not last:
                    pick(r + 1, 1 - par, 1)
                layer2(r)

            with pe.Fori(1, ROUNDS - 1, 2) as r:
                round_(r, 1)
                round_(r + 1, 0)
            round_(ROUNDS - 1, 1, last=True)
            pe.wait_ge(y_copied, ROUNDS - 1)
            layer3(ROUNDS - 1)


def layout(inputs):
    import numpy as np
    ids = np.asarray(inputs["ids"])
    tbl = [np.asarray(inputs[f"tbl_{f}"]) for f in range(F)]
    start = np.cumsum([0] + [ROWS[f] for f in SLOTS])[:F].astype(np.float32)

    def by_gather(a):
        return np.ascontiguousarray(a.reshape(-1, P).T)

    row_ids = np.concatenate([by_gather(ids[:RB, SLOTS]), by_gather(ids[RB:, SLOTS[:GF]])], axis=1)
    starts = np.concatenate([
        by_gather(np.broadcast_to(start, (RB, F))), by_gather(np.broadcast_to(start[:GF], (RB, GF)))], axis=1)

    w_top1 = np.asarray(inputs["W_top1"])
    place = np.zeros((F, F), np.int64)
    iu, ju = np.triu_indices(F, k=1)
    place[iu, ju] = place[ju, iu] = np.arange(len(iu))
    w1 = np.zeros((JQ, 32, JC, H1), w_top1.dtype)
    for a in range(F):
        for j in range(a + 1, F):
            w1[j // JC, a, j % JC] = w_top1[place[SLOTS[a], SLOTS[j]]]
    w1[0, 16:16 + CTX, 0] = w_top1[len(iu):]
    small = np.concatenate([np.asarray(inputs["b_top1"]).reshape(N1, P).T,
                            np.asarray(inputs["b_top2"]).reshape(N2, P).T,
                            np.asarray(inputs["W_top3"]).reshape(N2, P).T], axis=1)
    return {
        "row_ids": row_ids,
        "starts": starts,
        "pick_ids": np.ascontiguousarray(ids[:, PICKED].T).reshape(1, PICK * B),
        "tables": np.concatenate([tbl[f] for f in SLOTS]),
        "picked": np.stack([tbl[f] for f in PICKED]).reshape(PICK, KP, KR * D),
        "dense_t": np.ascontiguousarray(np.asarray(inputs["dense_ctx"]).T),
        "w1": w1.reshape(P, JC, H1),
        "w2": np.asarray(inputs["W_top2"]),
        "small": np.ascontiguousarray(small),
    }


def kernel(**inputs):
    import concourse.bacc as bacc
    from concourse.bass_utils import run_bass_kernel_spmd
    nc = bacc.Bacc("TRN2", target_bir_lowering=False, num_devices=1)
    arrays = layout(inputs)
    aps = [nc.dram_tensor(n, a.shape, mybir.dt.from_np(a.dtype), kind="ExternalInput").ap()
           for n, a in arrays.items()]
    y = nc.dram_tensor("y", (B, 1), mybir.dt.float32, kind="ExternalOutput").ap()
    build(nc, *aps, y)
    return run_bass_kernel_spmd(nc, [arrays], core_ids=[0]).results[0]["y"]
```

```python
import concourse.bass as bass
from concourse import mybir
from contextlib import ExitStack

P = 128
B, F, D = 512, 32, 128
RB = 64
ROUNDS = B // RB
UNITS = 4
UB = RB // UNITS
ROWS = [1000, 1250, 1250, 125000, 12500, 1000, 12500, 12500, 12500, 12500, 1250, 1000, 1000, 1000,
        1250, 12500, 1250, 1250, 1250, 12500, 12500, 1000, 1000, 1000, 1250, 1250, 1000, 1000,
        1000, 1250, 1250, 1250]
PICK = 8
PICK_ROWS = 1000
PICKED = [f for f in range(F) if ROWS[f] == PICK_ROWS][:PICK]
SLOTS = [f for f in range(F) if f not in PICKED] + PICKED
GF = F - PICK
GA = UB * F // P
G = UB * GF // P
LAST = ROUNDS - 1
DB = 2 * RB
KP = 125
KR = PICK_ROWS // KP
JQ, JC = 4, 8
CTX = 16
H1, H2 = 512, 256
N1, N2 = H1 // P, H2 // P
IDS0, IDS = 0, UNITS * GA
IDS_LAST = IDS + (ROUNDS - 2) * UNITS * G
START_ALL = IDS_LAST + UNITS * GA
START = START_ALL + UNITS * GA
IDCOLS = START + UNITS * G


def build(nc, row_ids, pick_ids, tables, picked, context, w1, w2, small, y):
    f32, bf16, i32 = mybir.dt.float32, mybir.dt.bfloat16, mybir.dt.int32
    ALU = mybir.AluOpType
    ACT = mybir.ActivationFunctionType
    ctx = ExitStack()
    with ctx:
        def sb(name, shape, dt):
            return ctx.enter_context(nc.sbuf_tensor(name, shape, dt))

        def pb(name, shape):
            return ctx.enter_context(nc.psum_tensor(name, shape, f32))

        def sem(name):
            return ctx.enter_context(nc.semaphore(name))

        ident = sb("ident", [P, P], f32)
        gate = sb("gate", [1, 3], f32)
        id_sb = sb("id_sb", [P, IDCOLS], i32)
        row_no = sb("row_no", [P, 2, UNITS * GA], i32)
        rows = sb("rows", [P, 2, UNITS * GA, D], f32)
        emb = sb("emb", [P, 2, RB, F], f32)
        pick_id_sb = sb("pick_id_sb", [KP, PICK, B], i32)
        pick_row = sb("pick_row", [KP, KR], i32)
        onehot = sb("onehot", [KP, 2, PICK, KR, RB], bf16)
        table = sb("table", [KP, PICK, KR * D], f32)
        rest = sb("rest", [KP, PICK, KR * D], f32)
        low = sb("low", [KP, PICK, KR * D], bf16)
        feat = sb("feat", [P, JC, B], f32)
        w1_sb = sb("w1_sb", [P, JC, H1], f32)
        w2_sb = sb("w2_sb", [P, N1, H2], f32)
        small_sb = sb("small_sb", [P, N1 + 2 * N2], f32)
        h1 = sb("h1", [P, N1, DB], f32)
        h2 = sb("h2", [P, N2, DB], f32)
        y_row = sb("y_row", [1, B], f32)
        b1 = small_sb[:, 0:N1]
        b2 = small_sb[:, N1:N1 + N2]
        w3 = small_sb[:, N1 + N2:N1 + 2 * N2]
        starts = id_sb[:, START_ALL:IDCOLS].bitcast(f32)
        table_hi = table[:, :, :].bitcast(bf16).rearrange("p t (n two) -> p t n two", two=2)[:, :, :, 1]
        rest_hi = rest[:, :, :].bitcast(bf16).rearrange("p t (n two) -> p t n two", two=2)[:, :, :, 1]
        parts = [table_hi, rest_hi, low[:, :, :]]

        turn_ps = [pb(f"turn_ps{i}", [P, 512]) for i in range(2)]
        dot_ps = [pb(f"dot_ps{i}", [P, RB // 4, F]) for i in range(2)]
        pick_ps = pb("pick_ps", [P, PICK, RB])
        h1_ps = [pb(f"h1_ps{i}", [P, N1 // 2, DB]) for i in range(2)]
        h2_ps = pb("h2_ps", [P, 512])

        ids_in = sem("ids_in")
        pick_ids_in = [sem(f"pick_ids_in{h}") for h in range(2)]
        table_in = [sem(f"table_in{t}") for t in range(PICK)]
        context_in = sem("context_in")
        weights_in = sem("weights_in")
        rows_in = [[sem(f"rows_in{p}_{u}") for u in range(UNITS)] for p in range(2)]
        stored = sem("stored")
        ident_ready = sem("ident_ready")
        pick_row_ready = sem("pick_row_ready")
        row_no_ready = sem("row_no_ready")
        gate_passed = sem("gate_passed")
        rest_ready = sem("rest_ready")
        low_ready = sem("low_ready")
        turned = sem("turned")
        emb_ready = sem("emb_ready")
        onehot_ready = sem("onehot_ready")
        picked_done = sem("picked_done")
        pick_emb_ready = sem("pick_emb_ready")
        dots = sem("dots")
        feat_act = sem("feat_act")
        feat_dve = sem("feat_dve")
        h1_done = sem("h1_done")
        h1_act = sem("h1_act")
        h1_dve = sem("h1_dve")
        h2_done = sem("h2_done")
        h2_ready = sem("h2_ready")
        y_done = sem("y_done")
        y_copied = sem("y_copied")

        feat_v = feat[:, :, :].rearrange("p c (g s) -> p c g s", s=4)

        def gathers(full):
            return GA if full else G

        def copy_dots(copy, r, par, quads):
            last = None
            for s in quads:
                for q in range(JQ):
                    n = 16 if q == 0 else 32
                    src = dot_ps[par][32 * s:32 * s + n, :, JC * q:JC * (q + 1)]
                    last = copy(feat_v[32 * q:32 * q + n, :, bass.ds(r * (RB // 4), RB // 4), s],
                                src.rearrange("p g c -> p c g"))
            return last

        block = ctx.enter_context(nc.Block())

        @block.sync
        def _(sp):
            sp.dma_start(id_sb[:, :], row_ids).then_inc(ids_in, 16)
            half = PICK // 2
            for t in range(PICK):
                if t >= 3:
                    sp.wait_ge(table_in[t - 3], 16)
                sp.dma_start(table[:, t, :], picked[t]).then_inc(table_in[t], 16)
                if t in (1, half):
                    h = t // half
                    sp.dma_start(pick_id_sb[:, half * h:half * (h + 1), :].rearrange("p t b -> p (t b)"),
                                 pick_ids[:, half * h * B:half * (h + 1) * B].broadcast_to([KP, half * B])
                                 ).then_inc(pick_ids_in[h], 16)
            sp.dma_start(feat[16:16 + CTX, :, :], context).then_inc(context_in, 16)
            for u in range(UNITS):
                sp.wait_ge(turned, u + 1)
                c = JC // UNITS
                sp.dma_start(w1_sb[:, c * u:c * (u + 1), :], w1[:, c * u:c * (u + 1), :]).then_inc(weights_in, 16)
            sp.dma_start(small_sb[:, :], small).then_inc(weights_in, 16)
            sp.dma_start(w2_sb[:, :, :], w2.rearrange("(c p) n -> p c n", p=P)).then_inc(weights_in, 16)
            sp.wait_ge(y_copied, ROUNDS // 2)
            sp.dma_start(y.rearrange("b o -> o b"), y_row[:, :]).then_inc(stored, 16)
            sp.wait_ge(stored, 16)

        @block.gpsimd
        def _(pool):
            def gather_round(r, par, full=False):
                pool.wait_ge(row_no_ready, r + 1)
                pool.tensor_tensor(gate[:, par:par + 1], gate[:, 2:3], gate[:, 2:3],
                                   ALU.add).then_inc(gate_passed, 1)
                n = gathers(full)
                for u in range(UNITS):
                    for c in range(n):
                        pool.indirect_dma_start(
                            rows[:, par, n * u + c, :], None, tables,
                            bass.IndirectOffsetOnAxis(ap=row_no[:, par, n * u + c:n * u + c + 1], axis=0)
                        ).then_inc(rows_in[par][u], 16)

            pool.memset(ident[:, :], 0.0).then_inc(ident_ready, 1)
            pool.iota(pick_row[:, :], [[1, KR]], base=0, channel_multiplier=KR).then_inc(pick_row_ready, 1)
            pool.memset(gate[:, :], 0.0).then_inc(ident_ready, 1)
            pool.wait_ge(ident_ready, 2)
            pool.affine_select(out=ident[:, :], in_=ident[:, :], compare_op=ALU.not_equal, fill=1.0,
                               base=0, pattern=[[-1, P]], channel_multiplier=1).then_inc(ident_ready, 1)
            gather_round(0, 0, full=True)
            with pool.Fori(1, LAST, 2) as r:
                gather_round(r, 1)
                gather_round(r + 1, 0)
            gather_round(LAST, 1, full=True)

        @block.vector
        def _(dve):
            def row_numbers(r, par):
                if isinstance(r, int) and r in (0, LAST):
                    at, n, start = (IDS_LAST if r else IDS0), UNITS * GA, 0
                else:
                    at, n, start = IDS + (r - 1) * (UNITS * G), UNITS * G, UNITS * GA
                if not isinstance(r, int) or r > 1:
                    dve.wait_ge(gate_passed, r - 1)
                dve.tensor_tensor(row_no[:, par, 0:n], id_sb[:, bass.ds(at, n)], starts[:, start:start + n],
                                  ALU.add).then_inc(row_no_ready, 1)

            def split(t):
                dve.wait_ge(table_in[t], 16)
                dve.tensor_tensor(rest[:, t, :], table[:, t, :], table_hi[:, t, :],
                                  ALU.subtract).then_inc(rest_ready, 1)
                dve.wait_ge(rest_ready, t + 1)
                dve.tensor_tensor(low[:, t, :], rest[:, t, :], rest_hi[:, t, :],
                                  ALU.subtract).then_inc(low_ready, 1)

            def make_onehot(r, par, half):
                n = PICK // 2
                ts = slice(n * half, n * half + n)
                ids = pick_id_sb[:, ts, bass.ds(r * RB, RB)]
                dve.tensor_tensor(onehot[:, par, ts, :, :],
                                  ids.unsqueeze(2).broadcast_to([KP, n, KR, RB]),
                                  pick_row[:, :].unsqueeze(1).unsqueeze(3).broadcast_to([KP, n, KR, RB]),
                                  ALU.is_equal).then_inc(onehot_ready, 1)

            def relu(out, sums, bias, n):
                return dve.tensor_scalar(out, sums, bias[:, n:n + 1], 0.0, ALU.add, ALU.max)

            def h1_relu(pair):
                dve.wait_ge(h1_done, pair + 1)
                for n in range(N1 // 2, N1):
                    last = relu(h1[:, n, :], h1_ps[1][:, n - N1 // 2, :], b1, n)
                last.then_inc(h1_dve, 1)

            def h2_relu(pair):
                dve.wait_ge(h2_done, pair + 1)
                for n in range(N2):
                    last = relu(h2[:, n, :], h2_ps[:, n * DB:(n + 1) * DB], b2, n)
                last.then_inc(h2_ready, 1)

            def dots_out(r, par):
                dve.wait_ge(dots, UNITS * r + UNITS)
                copy_dots(dve.tensor_copy, r, par, (2, 3)).then_inc(feat_dve, 1)

            dve.wait_ge(ids_in, 16)
            row_numbers(0, 0)
            row_numbers(1, 1)
            split(0)
            split(1)
            dve.wait_ge(pick_row_ready, 1)
            for half in range(2):
                dve.wait_ge(pick_ids_in[half], 16)
                make_onehot(1, 1, half)
                for t in range(2 + 2 * half, 4 + 4 * half):
                    split(t)
            dots_out(0, 0)
            row_numbers(2, 0)

            def round_(r, par, pair=None, onehots=True, numbers=True):
                if pair is not None:
                    h1_relu(pair)
                if onehots:
                    make_onehot(r + 1, 1 - par, 0)
                if pair is not None:
                    h2_relu(pair)
                if onehots:
                    make_onehot(r + 1, 1 - par, 1)
                dots_out(r, par)
                if numbers:
                    row_numbers(r + 2, par)

            with dve.Fori(0, 2) as i:
                round_(2 * i + 1, 1)
                round_(2 * i + 2, 0, pair=i)
            round_(5, 1)
            round_(6, 0, pair=2, onehots=False, numbers=False)
            dots_out(LAST, 1)
            h1_relu(3)
            h2_relu(3)

        @block.scalar
        def _(act):
            def emb_out(r, par, u, full=False):
                act.wait_ge(turned, UNITS * r + u + 1)
                n = F if full else GF
                act.activation(emb[:, par, UB * u:UB * (u + 1), 0:n],
                               turn_ps[u % 2][:, 0:UB * n].rearrange("p (b f) -> p b f", f=n),
                               ACT.Copy).then_inc(emb_ready, 1)

            def pick_out(r, par):
                act.wait_ge(picked_done, 2 * r)
                act.activation(emb[:, par, :, GF:F].rearrange("p b t -> p t b"), pick_ps[:, :, :],
                               ACT.Copy).then_inc(pick_emb_ready, 1)

            def dots_out(r, par):
                act.wait_ge(dots, UNITS * r + UNITS)
                copy_dots(lambda o, i: act.activation(o, i, ACT.Copy), r, par, (0, 1)).then_inc(feat_act, 1)

            def h1_relu(pair):
                act.wait_ge(h1_done, pair + 1)
                for n in range(N1 // 2):
                    last = act.activation(h1[:, n, :], h1_ps[0][:, n, :], ACT.Relu, bias=b1[:, n:n + 1])
                last.then_inc(h1_act, 1)

            def y_out(pair):
                act.wait_ge(y_done, pair + 1)
                act.activation(y_row[:, bass.ds(pair * DB, DB)], h2_ps[0:1, 2 * DB:3 * DB],
                               ACT.Copy).then_inc(y_copied, 1)

            def round_(r, par, pair=None, full=False):
                if pair is not None:
                    h1_relu(pair)
                if not full:
                    pick_out(r, par)
                for u in range(UNITS):
                    emb_out(r, par, u, full)
                    if u == 0 and pair is not None:
                        y_out(pair)
                dots_out(r, par)

            round_(0, 0, full=True)
            with act.Fori(0, 2) as i:
                round_(2 * i + 1, 1)
                round_(2 * i + 2, 0, pair=i)
            round_(5, 1)
            round_(6, 0, pair=2)
            round_(LAST, 1, full=True)
            h1_relu(3)
            y_out(3)

        @block.tensor
        def _(pe):
            def turn(r, par, u, full=False):
                n = gathers(full)
                landed = 24 * r + (64 if par == 0 else 40 if full else 24)
                pe.wait_ge(rows_in[par][u], landed)
                for c in range(n):
                    last = pe.transpose(turn_ps[u % 2][:, c * P:(c + 1) * P],
                                        rows[:, par, n * u + c, :], ident[:, :])
                last.then_inc(turned, 1)

            def dot(r, par, u):
                pe.wait_ge(emb_ready, UNITS * r + u + 1)
                for b in range(UB * u, UB * (u + 1)):
                    s, g = b % 4, b // 4
                    e = emb[:, par, b, :]
                    last = pe.matmul(dot_ps[par][32 * s:32 * s + 32, g, :], e, e, start=True, stop=True,
                                     tile_position=(0, 32 * s))
                last.then_inc(dots, 1)

            def pick(r, par, half, first=False):
                pe.wait_ge(onehot_ready, 2 * r + half - 1)
                n = PICK // 2
                for t in range(n * half, n * half + n):
                    if first:
                        pe.wait_ge(low_ready, t + 1)
                    for k in range(KR):
                        for m, part in enumerate(parts):
                            last = pe.matmul(pick_ps[:, t, :], part[:, t, D * k:D * (k + 1)],
                                             onehot[:, par, t, k, :], start=(k == 0 and m == 0),
                                             stop=(k == KR - 1 and m == len(parts) - 1))
                last.then_inc(picked_done, 1)

            def layer1(pair):
                pe.wait_ge(feat_act, 2 * pair + 2)
                pe.wait_ge(feat_dve, 2 * pair + 2)
                for n in range(N1):
                    for c in range(JC):
                        last = pe.matmul(h1_ps[n // 2][:, n % 2, :], w1_sb[:, c, n * P:(n + 1) * P],
                                         feat[:, c, bass.ds(pair * DB, DB)], start=(c == 0), stop=(c == JC - 1))
                last.then_inc(h1_done, 1)

            def layer2(pair):
                pe.wait_ge(h1_act, pair + 1)
                pe.wait_ge(h1_dve, pair + 1)
                for n in range(N2):
                    for c in range(N1):
                        last = pe.matmul(h2_ps[:, n * DB:(n + 1) * DB], w2_sb[:, c, n * P:(n + 1) * P],
                                         h1[:, c, :], start=(c == 0), stop=(c == N1 - 1))
                last.then_inc(h2_done, 1)

            def layer3(pair):
                pe.wait_ge(h2_ready, pair + 1)
                for c in range(N2):
                    last = pe.matmul(h2_ps[0:1, 2 * DB:3 * DB], w3[:, c:c + 1], h2[:, c, :],
                                     start=(c == 0), stop=(c == N2 - 1))
                last.then_inc(y_done, 1)

            def turn_and_dot(r, par, pair=None, full=False):
                turn(r, par, 0, full)
                if pair is not None:
                    layer3(pair)
                turn(r, par, 1, full)
                if not full:
                    pe.wait_ge(pick_emb_ready, r)
                dot(r, par, 0)
                turn(r, par, 2, full)
                dot(r, par, 1)
                turn(r, par, 3, full)
                dot(r, par, 2)
                dot(r, par, 3)

            def two_rounds(r, pair, picks=True):
                turn_and_dot(r, 1)
                pick(r + 1, 0, 0)
                layer1(pair)
                pick(r + 1, 0, 1)
                layer2(pair)
                turn_and_dot(r + 1, 0, pair)
                if picks:
                    pick(r + 2, 1, 0)
                    pick(r + 2, 1, 1)

            pe.wait_ge(ident_ready, 3)
            turn_and_dot(0, 0, full=True)
            pick(1, 1, 0, first=True)
            pick(1, 1, 1, first=True)
            pe.wait_ge(context_in, 16)
            pe.wait_ge(weights_in, 96)
            with pe.Fori(0, 2) as i:
                two_rounds(2 * i + 1, i)
            two_rounds(5, 2, picks=False)
            turn_and_dot(LAST, 1, full=True)
            layer1(3)
            layer2(3)
            layer3(3)


def layout(inputs):
    import numpy as np
    ids = np.asarray(inputs["ids"])
    tbl = [np.asarray(inputs[f"tbl_{f}"]) for f in range(F)]
    start = np.cumsum([0] + [ROWS[f] for f in SLOTS])[:F].astype(np.float32)

    def by_gather(a):
        return np.ascontiguousarray(a.reshape(-1, P).T)

    starts = np.concatenate([
        by_gather(np.broadcast_to(start, (RB, F))), by_gather(np.broadcast_to(start[:GF], (RB, GF)))], axis=1)
    row_ids = np.concatenate([
        by_gather(ids[:RB, SLOTS]), by_gather(ids[RB:-RB, SLOTS[:GF]]), by_gather(ids[-RB:, SLOTS]),
        starts.view(ids.dtype)], axis=1)
    context = np.zeros((CTX, JC, B), np.float32)
    context[:, 0] = np.asarray(inputs["dense_ctx"]).T

    w_top1 = np.asarray(inputs["W_top1"])
    place = np.zeros((F, F), np.int64)
    iu, ju = np.triu_indices(F, k=1)
    place[iu, ju] = place[ju, iu] = np.arange(len(iu))
    w1 = np.zeros((JQ, 32, JC, H1), w_top1.dtype)
    for a in range(F):
        for j in range(a + 1, F):
            w1[j // JC, a, j % JC] = w_top1[place[SLOTS[a], SLOTS[j]]]
    w1[0, 16:16 + CTX, 0] = w_top1[len(iu):]
    small = np.concatenate([np.asarray(inputs["b_top1"]).reshape(N1, P).T,
                            np.asarray(inputs["b_top2"]).reshape(N2, P).T,
                            np.asarray(inputs["W_top3"]).reshape(N2, P).T], axis=1)
    return {
        "row_ids": row_ids,
        "pick_ids": np.ascontiguousarray(ids[:, PICKED].T).reshape(1, PICK * B),
        "tables": np.concatenate([tbl[f] for f in SLOTS]),
        "picked": np.stack([tbl[f] for f in PICKED]).reshape(PICK, KP, KR * D),
        "context": context,
        "w1": w1.reshape(P, JC, H1),
        "w2": np.asarray(inputs["W_top2"]),
        "small": np.ascontiguousarray(small),
    }


def kernel(**inputs):
    import concourse.bacc as bacc
    from concourse.bass_utils import run_bass_kernel_spmd
    nc = bacc.Bacc("TRN2", target_bir_lowering=False, num_devices=1)
    arrays = layout(inputs)
    aps = [nc.dram_tensor(n, a.shape, mybir.dt.from_np(a.dtype), kind="ExternalInput").ap()
           for n, a in arrays.items()]
    y = nc.dram_tensor("y", (B, 1), mybir.dt.float32, kind="ExternalOutput").ap()
    build(nc, *aps, y)
    return run_bass_kernel_spmd(nc, [arrays], core_ids=[0]).results[0]["y"]
```

```python
import concourse.bass as bass
from concourse import mybir
from contextlib import ExitStack

P = 128
B, F, D = 512, 32, 128
RB = 64
ROUNDS = B // RB
UNITS = 4
UB = RB // UNITS
ROWS = [1000, 1250, 1250, 125000, 12500, 1000, 12500, 12500, 12500, 12500, 1250, 1000, 1000, 1000,
        1250, 12500, 1250, 1250, 1250, 12500, 12500, 1000, 1000, 1000, 1250, 1250, 1000, 1000,
        1000, 1250, 1250, 1250]
PICK = 8
PICK_ROWS = 1000
PICKED = [f for f in range(F) if ROWS[f] == PICK_ROWS][:PICK]
SLOTS = [f for f in range(F) if f not in PICKED] + PICKED
GF = F - PICK
GA = UB * F // P
G = UB * GF // P
LAST = ROUNDS - 1
DB = 2 * RB
KP = 125
KR = PICK_ROWS // KP
JQ, JC = 4, 8
CTX = 16
H1, H2 = 512, 256
N1, N2 = H1 // P, H2 // P
IDS0, IDS = 0, UNITS * GA
IDS_LAST = IDS + (ROUNDS - 2) * UNITS * G
START_ALL = IDS_LAST + UNITS * GA
START = START_ALL + UNITS * GA
IDCOLS = START + UNITS * G


def build(nc, row_ids, pick_ids, tables, picked, context, w1, w2, small, y):
    f32, bf16, i32 = mybir.dt.float32, mybir.dt.bfloat16, mybir.dt.int32
    f16 = mybir.dt.float16
    ALU = mybir.AluOpType
    ACT = mybir.ActivationFunctionType
    ctx = ExitStack()
    with ctx:
        def sb(name, shape, dt):
            return ctx.enter_context(nc.sbuf_tensor(name, shape, dt))

        def pb(name, shape):
            return ctx.enter_context(nc.psum_tensor(name, shape, f32))

        def sem(name):
            return ctx.enter_context(nc.semaphore(name))

        ident = sb("ident", [P, P], f32)
        gate = sb("gate", [1, 3], f32)
        id_sb = sb("id_sb", [P, IDCOLS], i32)
        row_no = sb("row_no", [P, 3, UNITS * GA], i32)
        rows = sb("rows", [P, 3, UNITS * GA, D], f32)
        emb = sb("emb", [P, 2, RB, F], f32)
        pick_id_sb = sb("pick_id_sb", [KP, PICK, B], i32)
        pick_row_sb = sb("pick_row_sb", [KP, KR, RB], i32)
        pick_id = sb("pick_id", [KP, PICK, B], f16)
        pick_row = sb("pick_row", [KP, KR, RB], f16)
        onehot = sb("onehot", [KP, 2, PICK, KR, RB], bf16)
        table = sb("table", [KP, PICK, KR * D], f32)
        rest = sb("rest", [KP, PICK, KR * D], f32)
        low = sb("low", [KP, PICK, KR * D], bf16)
        feat = sb("feat", [P, JC, B], f32)
        w1_sb = sb("w1_sb", [P, JC, H1], f32)
        w2_sb = sb("w2_sb", [P, N1, H2], f32)
        small_sb = sb("small_sb", [P, N1 + 2 * N2], f32)
        h1 = sb("h1", [P, N1, DB], f32)
        h2 = sb("h2", [P, N2, DB], f32)
        y_row = sb("y_row", [1, B], f32)
        b1 = small_sb[:, 0:N1]
        b2 = small_sb[:, N1:N1 + N2]
        w3 = small_sb[:, N1 + N2:N1 + 2 * N2]
        starts = id_sb[:, START_ALL:IDCOLS].bitcast(f32)
        table_hi = table[:, :, :].bitcast(bf16).rearrange("p t (n two) -> p t n two", two=2)[:, :, :, 1]
        rest_hi = rest[:, :, :].bitcast(bf16).rearrange("p t (n two) -> p t n two", two=2)[:, :, :, 1]
        parts = [table_hi, rest_hi, low[:, :, :]]

        turn_ps = [pb(f"turn_ps{i}", [P, 512]) for i in range(2)]
        dot_ps = pb("dot_ps", [P, RB // 4, 2 * F])
        pick_ps = pb("pick_ps", [P, PICK, RB])
        h1_ps = [pb(f"h1_ps{i}", [P, N1 // 2, DB]) for i in range(2)]
        h2_ps = pb("h2_ps", [P, 512])

        ids_in = sem("ids_in")
        pick_ids_in = [sem(f"pick_ids_in{h}") for h in range(2)]
        table_in = [sem(f"table_in{t}") for t in range(PICK)]
        context_in = sem("context_in")
        weights_in = sem("weights_in")
        rows_in = [[sem(f"rows_in{p}_{u}") for u in range(UNITS)] for p in range(3)]
        stored = sem("stored")
        ident_ready = sem("ident_ready")
        pick_rows_made = sem("pick_rows_made")
        pick_row_ready = sem("pick_row_ready")
        pick_id_ready = sem("pick_id_ready")
        row_no_ready = sem("row_no_ready")
        last_row_no_ready = sem("last_row_no_ready")
        gate_passed = sem("gate_passed")
        rest_ready = sem("rest_ready")
        low_ready = sem("low_ready")
        turned = sem("turned")
        emb_ready = sem("emb_ready")
        onehot_ready = sem("onehot_ready")
        picked_done = sem("picked_done")
        pick_emb_ready = sem("pick_emb_ready")
        dots = sem("dots")
        feat_act = sem("feat_act")
        feat_dve = sem("feat_dve")
        h1_done = sem("h1_done")
        h1_act = sem("h1_act")
        h1_dve = sem("h1_dve")
        h2_done = sem("h2_done")
        h2_ready = sem("h2_ready")
        last_h2_done = sem("last_h2_done")
        last_h2_act = sem("last_h2_act")
        y_done = sem("y_done")
        y_copied = sem("y_copied")

        feat_v = feat[:, :, :].rearrange("p c (g s) -> p c g s", s=4)

        def gathers(full):
            return GA if full else G

        def copy_dots(copy, r, quads, groups):
            last = None
            g0, gn = groups
            for s in quads:
                for q in range(JQ):
                    n = 16 if q == 0 else 32
                    j = F * (s % 2) + JC * q
                    src = dot_ps[32 * s:32 * s + n, g0:g0 + gn, j:j + JC]
                    last = copy(feat_v[32 * q:32 * q + n, :, bass.ds(r * (RB // 4) + g0, gn), s],
                                src.rearrange("p g c -> p c g"))
            return last

        block = ctx.enter_context(nc.Block())

        @block.sync
        def _(sp):
            sp.dma_start(id_sb[:, :], row_ids).then_inc(ids_in, 16)
            half = PICK // 2
            for t in range(PICK):
                if t >= 3:
                    sp.wait_ge(table_in[t - 3], 16)
                sp.dma_start(table[:, t, :], picked[t]).then_inc(table_in[t], 16)
                if t in (1, half):
                    h = t // half
                    sp.dma_start(pick_id_sb[:, half * h:half * (h + 1), :].rearrange("p t b -> p (t b)"),
                                 pick_ids[:, half * h * B:half * (h + 1) * B].broadcast_to([KP, half * B])
                                 ).then_inc(pick_ids_in[h], 16)
            sp.dma_start(feat[16:16 + CTX, :, :], context).then_inc(context_in, 16)
            for u in range(UNITS):
                sp.wait_ge(turned, u + 1)
                c = JC // UNITS
                sp.dma_start(w1_sb[:, c * u:c * (u + 1), :], w1[:, c * u:c * (u + 1), :]).then_inc(weights_in, 16)
            sp.dma_start(small_sb[:, :], small).then_inc(weights_in, 16)
            sp.dma_start(w2_sb[:, :, :], w2.rearrange("(c p) n -> p c n", p=P)).then_inc(weights_in, 16)
            sp.wait_ge(y_copied, ROUNDS // 2)
            sp.dma_start(y.rearrange("b o -> o b"), y_row[:, :]).then_inc(stored, 16)
            sp.wait_ge(stored, 16)

        @block.gpsimd
        def _(pool):
            def gather_round(r, par, full=False):
                if isinstance(r, int):
                    pool.wait_ge(row_no_ready if par < 2 else last_row_no_ready, 1)
                else:
                    pool.wait_ge(row_no_ready, r + 1)
                    pool.tensor_tensor(gate[:, par:par + 1], gate[:, 2:3], gate[:, 2:3],
                                       ALU.add).then_inc(gate_passed, 1)
                n = gathers(full)
                for u in range(UNITS):
                    for c in range(n):
                        pool.indirect_dma_start(
                            rows[:, par, n * u + c, :], None, tables,
                            bass.IndirectOffsetOnAxis(ap=row_no[:, par, n * u + c:n * u + c + 1], axis=0)
                        ).then_inc(rows_in[par][u], 16)

            pool.memset(ident[:, :], 0.0).then_inc(ident_ready, 1)
            pool.iota(pick_row_sb[:, :, :], [[1, KR], [0, RB]], base=0,
                      channel_multiplier=KR).then_inc(pick_rows_made, 1)
            pool.memset(gate[:, :], 0.0).then_inc(ident_ready, 1)
            pool.wait_ge(ident_ready, 2)
            pool.affine_select(out=ident[:, :], in_=ident[:, :], compare_op=ALU.not_equal, fill=1.0,
                               base=0, pattern=[[-1, P]], channel_multiplier=1).then_inc(ident_ready, 1)
            gather_round(0, 0, full=True)
            with pool.Fori(1, LAST, 2) as r:
                gather_round(r, 1)
                gather_round(r + 1, 0)
            gather_round(LAST, 2, full=True)

        @block.vector
        def _(dve):
            def row_numbers(r, par, ready=row_no_ready):
                if isinstance(r, int) and r in (0, LAST):
                    at, n, start = (IDS_LAST if r else IDS0), UNITS * GA, 0
                else:
                    at, n, start = IDS + (r - 1) * (UNITS * G), UNITS * G, UNITS * GA
                if not isinstance(r, int) or r == 2:
                    dve.wait_ge(turned, UNITS * (r - 1))
                if not isinstance(r, int):
                    dve.wait_ge(gate_passed, r - 2)
                dve.tensor_tensor(row_no[:, par, 0:n], id_sb[:, bass.ds(at, n)], starts[:, start:start + n],
                                  ALU.add).then_inc(ready, 1)

            def split(t):
                dve.wait_ge(table_in[t], 16)
                dve.tensor_tensor(rest[:, t, :], table[:, t, :], table_hi[:, t, :],
                                  ALU.subtract).then_inc(rest_ready, 1)
                dve.wait_ge(rest_ready, t + 1)
                dve.tensor_tensor(low[:, t, :], rest[:, t, :], rest_hi[:, t, :],
                                  ALU.subtract).then_inc(low_ready, 1)

            def make_onehot(r, par, half):
                if not isinstance(r, int):
                    dve.wait_ge(picked_done, 2 * r - 5 + half)
                n = PICK // 2
                ts = slice(n * half, n * half + n)
                ids = pick_id[:, ts, bass.ds(r * RB, RB)]
                dve.tensor_tensor(onehot[:, par, ts, :, :],
                                  ids.unsqueeze(2).broadcast_to([KP, n, KR, RB]),
                                  pick_row[:, :, :].unsqueeze(1).broadcast_to([KP, n, KR, RB]),
                                  ALU.is_equal).then_inc(onehot_ready, 1)

            def relu(out, sums, bias, n):
                return dve.tensor_scalar(out, sums, bias[:, n:n + 1], 0.0, ALU.add, ALU.max)

            def h1_relu(pair, n):
                dve.wait_ge(h1_done, N1 * pair + n + 1)
                relu(h1[:, n, :], h1_ps[n % 2][:, n // 2, :], b1, n).then_inc(h1_dve, 1)

            def h2_relu(pair):
                dve.wait_ge(h2_done, pair + 1)
                for n in range(N2):
                    last = relu(h2[:, n, :], h2_ps[:, n * DB:(n + 1) * DB], b2, n)
                last.then_inc(h2_ready, 1)

            def dots_out(r, half=None):
                if half == 0:
                    dve.wait_ge(dots, UNITS * r + UNITS // 2)
                    copy_dots(dve.tensor_copy, r, (2, 3), (0, RB // 8))
                else:
                    dve.wait_ge(dots, UNITS * r + UNITS)
                    copy_dots(dve.tensor_copy, r, (2, 3),
                              (RB // 8, RB // 8) if half else (0, RB // 4)).then_inc(feat_dve, 1)

            dve.wait_ge(ids_in, 16)
            row_numbers(0, 0)
            row_numbers(1, 1)
            row_numbers(LAST, 2, last_row_no_ready)
            for t in range(PICK):
                split(t)
                if t in (2, 5):
                    dve.wait_ge(pick_row_ready, 1)
                    dve.wait_ge(pick_id_ready, t // 3 + 1)
                    make_onehot(1, 1, t // 3)
            row_numbers(2, 0)
            make_onehot(2, 0, 0)
            make_onehot(2, 0, 1)
            dots_out(0)

            with dve.Fori(0, 2) as i:
                make_onehot(2 * i + 3, 1, 0)
                make_onehot(2 * i + 3, 1, 1)
                row_numbers(2 * i + 3, 1)
                dots_out(2 * i + 1)
                make_onehot(2 * i + 4, 0, 0)
                make_onehot(2 * i + 4, 0, 1)
                h1_relu(i, 1)
                row_numbers(2 * i + 4, 0)
                dots_out(2 * i + 2)
                h1_relu(i, 3)
                h2_relu(i)
            dots_out(5)
            dots_out(6)
            h1_relu(2, 1)
            h1_relu(2, 3)
            dots_out(LAST, 0)
            dots_out(LAST, 1)
            h2_relu(2)
            h1_relu(3, 1)
            h1_relu(3, 3)
            dve.wait_ge(last_h2_done, 2)
            relu(h2[:, 1, :], turn_ps[0][:, 0:DB], b2, 1).then_inc(h2_ready, 1)

        @block.scalar
        def _(act):
            def emb_out(r, par, u, full=False):
                act.wait_ge(turned, UNITS * r + u + 1)
                n = F if full else GF
                act.activation(emb[:, par, UB * u:UB * (u + 1), 0:n],
                               turn_ps[u % 2][:, 0:UB * n].rearrange("p (b f) -> p b f", f=n),
                               ACT.Copy).then_inc(emb_ready, 1)

            def pick_out(r, par):
                act.wait_ge(picked_done, 2 * r)
                act.activation(emb[:, par, :, GF:F].rearrange("p b t -> p t b"), pick_ps[:, :, :],
                               ACT.Copy).then_inc(pick_emb_ready, 1)

            def copy(out, in_):
                return act.activation(out, in_, ACT.Copy)

            def dots_out(r, half=None):
                if half == 0:
                    act.wait_ge(dots, UNITS * r + UNITS // 2)
                    copy_dots(copy, r, (0, 1), (0, RB // 8))
                else:
                    act.wait_ge(dots, UNITS * r + UNITS)
                    copy_dots(copy, r, (0, 1),
                              (RB // 8, RB // 8) if half else (0, RB // 4)).then_inc(feat_act, 1)

            def h1_relu(pair, n):
                act.wait_ge(h1_done, N1 * pair + n + 1)
                act.activation(h1[:, n, :], h1_ps[n % 2][:, n // 2, :], ACT.Relu,
                               bias=b1[:, n:n + 1]).then_inc(h1_act, 1)

            def y_out(pair):
                act.wait_ge(y_done, pair + 1)
                act.activation(y_row[:, bass.ds(pair * DB, DB)], h2_ps[0:1, 2 * DB:3 * DB],
                               ACT.Copy).then_inc(y_copied, 1)

            def embs_out(r, par, units, full=False):
                for u in units:
                    emb_out(r, par, u, full)

            act.wait_ge(pick_rows_made, 1)
            copy(pick_row[:, :, :], pick_row_sb[:, :, :]).then_inc(pick_row_ready, 1)
            for half in range(2):
                ts = slice(PICK // 2 * half, PICK // 2 * (half + 1))
                act.wait_ge(pick_ids_in[half], 16)
                copy(pick_id[:, ts, :], pick_id_sb[:, ts, :]).then_inc(pick_id_ready, 1)
            embs_out(0, 0, (0, 1, 2, 3), full=True)
            dots_out(0)
            pick_out(1, 1)
            embs_out(1, 1, (0, 1))
            pick_out(2, 0)
            with act.Fori(0, 2) as i:
                embs_out(2 * i + 1, 1, (2, 3))
                dots_out(2 * i + 1)
                h1_relu(i, 0)
                embs_out(2 * i + 2, 0, (0, 1))
                pick_out(2 * i + 3, 1)
                embs_out(2 * i + 2, 0, (2, 3))
                dots_out(2 * i + 2)
                h1_relu(i, 2)
                embs_out(2 * i + 3, 1, (0, 1))
                pick_out(2 * i + 4, 0)
                y_out(i)
            embs_out(5, 1, (2, 3))
            dots_out(5)
            embs_out(6, 0, (0, 1, 2, 3))
            dots_out(6)
            emb_out(LAST, 1, 0, full=True)
            h1_relu(2, 0)
            emb_out(LAST, 1, 1, full=True)
            h1_relu(2, 2)
            emb_out(LAST, 1, 2, full=True)
            dots_out(LAST, 0)
            emb_out(LAST, 1, 3, full=True)
            dots_out(LAST, 1)
            h1_relu(3, 0)
            y_out(2)
            h1_relu(3, 2)
            act.wait_ge(last_h2_done, 1)
            act.activation(h2[:, 0, :], h2_ps[:, 0:DB], ACT.Relu, bias=b2[:, 0:1]).then_inc(last_h2_act, 1)
            y_out(3)

        @block.tensor
        def _(pe):
            def turn(r, par, u, full=False):
                n = gathers(full)
                buf = 2 if isinstance(r, int) and r == LAST else par
                landed = 64 if buf == 2 else 24 * r + (64 if par == 0 else 24)
                pe.wait_ge(rows_in[buf][u], landed)
                if u >= 2:
                    pe.wait_ge(emb_ready, UNITS * r + u - 1)
                for c in range(n):
                    last = pe.transpose(turn_ps[u % 2][:, c * P:(c + 1) * P],
                                        rows[:, buf, n * u + c, :], ident[:, :])
                last.then_inc(turned, 1)

            def dot(r, par, u):
                pe.wait_ge(emb_ready, UNITS * r + u + 1)
                for b in range(UB * u, UB * (u + 1), 2):
                    s, g = b % 4, b // 4
                    e = emb[:, par, b:b + 2, :].rearrange("p b f -> p (b f)")
                    last = pe.matmul(dot_ps[32 * s:32 * s + 64, g, :], e, e, start=True, stop=True,
                                     tile_position=(0, 32 * s))
                last.then_inc(dots, 1)

            def pick(r, par, half, first=False):
                pe.wait_ge(onehot_ready, 2 * r + half - 1)
                if half == 0 and not first:
                    pe.wait_ge(pick_emb_ready, r - 1)
                n = PICK // 2
                for t in range(n * half, n * half + n):
                    if first:
                        pe.wait_ge(low_ready, t + 1)
                    for k in range(KR):
                        for m, part in enumerate(parts):
                            last = pe.matmul(pick_ps[:, t, :], part[:, t, D * k:D * (k + 1)],
                                             onehot[:, par, t, k, :], start=(k == 0 and m == 0),
                                             stop=(k == KR - 1 and m == len(parts) - 1))
                last.then_inc(picked_done, 1)

            def layer1(pair, half):
                if half == 0:
                    pe.wait_ge(feat_act, 2 * pair + 2)
                    pe.wait_ge(feat_dve, 2 * pair + 2)
                for n in (2 * half, 2 * half + 1):
                    if half == 1:
                        pe.wait_ge(h1_dve if n % 2 else h1_act, 2 * pair + 1)
                    for c in range(JC):
                        last = pe.matmul(h1_ps[n % 2][:, n // 2, :], w1_sb[:, c, n * P:(n + 1) * P],
                                         feat[:, c, bass.ds(pair * DB, DB)], start=(c == 0), stop=(c == JC - 1))
                    last.then_inc(h1_done, 1)

            def add_layer2(out, n, c):
                return pe.matmul(out, w2_sb[:, c, n * P:(n + 1) * P], h1[:, c, :],
                                 start=(c == 0), stop=(c == N1 - 1))

            def layer2(pair):
                pe.wait_ge(h1_act, 2 * pair + 2)
                pe.wait_ge(h1_dve, 2 * pair + 2)
                for n in range(N2):
                    for c in range(N1):
                        last = add_layer2(h2_ps[:, n * DB:(n + 1) * DB], n, c)
                last.then_inc(h2_done, 1)

            def last_layer2():
                outs = [h2_ps[:, 0:DB], turn_ps[0][:, 0:DB]]
                pe.wait_ge(y_copied, 3)
                pe.wait_ge(h1_act, 8)
                for c in range(N1):
                    if c == 1:
                        pe.wait_ge(h1_dve, 7)
                    if c == 3:
                        pe.wait_ge(h1_dve, 8)
                    for n in range(N2):
                        mm = add_layer2(outs[n], n, c)
                        if c == N1 - 1:
                            mm.then_inc(last_h2_done, 1)

            def last_layer3():
                y_ps = h2_ps[0:1, 2 * DB:3 * DB]
                pe.wait_ge(last_h2_act, 1)
                pe.matmul(y_ps, w3[:, 0:1], h2[:, 0, :], start=True, stop=False)
                pe.wait_ge(h2_ready, 4)
                pe.matmul(y_ps, w3[:, 1:2], h2[:, 1, :], start=False, stop=True).then_inc(y_done, 1)

            def layer3(pair):
                pe.wait_ge(h2_ready, pair + 1)
                for c in range(N2):
                    last = pe.matmul(h2_ps[0:1, 2 * DB:3 * DB], w3[:, c:c + 1], h2[:, c, :],
                                     start=(c == 0), stop=(c == N2 - 1))
                last.then_inc(y_done, 1)

            def dots_free(r):
                pe.wait_ge(feat_act, r)
                pe.wait_ge(feat_dve, r)

            def rest_of_round(r, par):
                pe.wait_ge(pick_emb_ready, r)
                turn(r, par, 2)
                turn(r, par, 3)
                dots_free(r)
                for u in range(UNITS):
                    dot(r, par, u)

            pe.wait_ge(ident_ready, 3)
            pick(1, 1, 0, first=True)
            turn(0, 0, 0, full=True)
            turn(0, 0, 1, full=True)
            dot(0, 0, 0)
            turn(0, 0, 2, full=True)
            dot(0, 0, 1)
            turn(0, 0, 3, full=True)
            dot(0, 0, 2)
            dot(0, 0, 3)
            pick(1, 1, 1, first=True)
            pick(2, 0, 0)
            turn(1, 1, 0)
            turn(1, 1, 1)
            pick(2, 0, 1)
            pe.wait_ge(context_in, 16)
            pe.wait_ge(weights_in, 96)
            with pe.Fori(0, 2) as i:
                rest_of_round(2 * i + 1, 1)
                pick(2 * i + 3, 1, 0)
                layer1(i, 0)
                turn(2 * i + 2, 0, 0)
                turn(2 * i + 2, 0, 1)
                pick(2 * i + 3, 1, 1)
                rest_of_round(2 * i + 2, 0)
                layer1(i, 1)
                pick(2 * i + 4, 0, 0)
                layer2(i)
                turn(2 * i + 3, 1, 0)
                turn(2 * i + 3, 1, 1)
                pick(2 * i + 4, 0, 1)
                layer3(i)
            rest_of_round(5, 1)
            turn(6, 0, 0)
            turn(6, 0, 1)
            rest_of_round(6, 0)
            turn(LAST, 1, 0, full=True)
            layer1(2, 0)
            turn(LAST, 1, 1, full=True)
            dots_free(LAST)
            dot(LAST, 1, 0)
            layer1(2, 1)
            turn(LAST, 1, 2, full=True)
            dot(LAST, 1, 1)
            dot(LAST, 1, 2)
            turn(LAST, 1, 3, full=True)
            dot(LAST, 1, 3)
            layer2(2)
            layer1(3, 0)
            layer3(2)
            layer1(3, 1)
            last_layer2()
            last_layer3()


def layout(inputs):
    import numpy as np
    ids = np.asarray(inputs["ids"])
    tbl = [np.asarray(inputs[f"tbl_{f}"]) for f in range(F)]
    start = np.cumsum([0] + [ROWS[f] for f in SLOTS])[:F].astype(np.float32)

    def by_gather(a):
        return np.ascontiguousarray(a.reshape(-1, P).T)

    starts = np.concatenate([
        by_gather(np.broadcast_to(start, (RB, F))), by_gather(np.broadcast_to(start[:GF], (RB, GF)))], axis=1)
    row_ids = np.concatenate([
        by_gather(ids[:RB, SLOTS]), by_gather(ids[RB:-RB, SLOTS[:GF]]), by_gather(ids[-RB:, SLOTS]),
        starts.view(ids.dtype)], axis=1)
    context = np.zeros((CTX, JC, B), np.float32)
    context[:, 0] = np.asarray(inputs["dense_ctx"]).T

    w_top1 = np.asarray(inputs["W_top1"])
    place = np.zeros((F, F), np.int64)
    iu, ju = np.triu_indices(F, k=1)
    place[iu, ju] = place[ju, iu] = np.arange(len(iu))
    w1 = np.zeros((JQ, 32, JC, H1), w_top1.dtype)
    for a in range(F):
        for j in range(a + 1, F):
            w1[j // JC, a, j % JC] = w_top1[place[SLOTS[a], SLOTS[j]]]
    w1[0, 16:16 + CTX, 0] = w_top1[len(iu):]
    small = np.concatenate([np.asarray(inputs["b_top1"]).reshape(N1, P).T,
                            np.asarray(inputs["b_top2"]).reshape(N2, P).T,
                            np.asarray(inputs["W_top3"]).reshape(N2, P).T], axis=1)
    return {
        "row_ids": row_ids,
        "pick_ids": np.ascontiguousarray(ids[:, PICKED].T).reshape(1, PICK * B),
        "tables": np.concatenate([tbl[f] for f in SLOTS]),
        "picked": np.stack([tbl[f] for f in PICKED]).reshape(PICK, KP, KR * D),
        "context": context,
        "w1": w1.reshape(P, JC, H1),
        "w2": np.asarray(inputs["W_top2"]),
        "small": np.ascontiguousarray(small),
    }


def kernel(**inputs):
    import concourse.bacc as bacc
    from concourse.bass_utils import run_bass_kernel_spmd
    nc = bacc.Bacc("TRN2", target_bir_lowering=False, num_devices=1)
    arrays = layout(inputs)
    aps = [nc.dram_tensor(n, a.shape, mybir.dt.from_np(a.dtype), kind="ExternalInput").ap()
           for n, a in arrays.items()]
    y = nc.dram_tensor("y", (B, 1), mybir.dt.float32, kind="ExternalOutput").ap()
    build(nc, *aps, y)
    return run_bass_kernel_spmd(nc, [arrays], core_ids=[0]).results[0]["y"]
```
